# Optimizing a Trainium2 kernel written in Bass

```python
import numpy as np
import jax
import jax.numpy as jnp

def _softmax(x, axis=-1):
    return jax.nn.softmax(x, axis=axis)

def _gelu(x):
    return jax.nn.gelu(x, approximate=True)

def _silu(x):
    return jax.nn.silu(x)

def _sigmoid(x):
    return jax.nn.sigmoid(x)

def _layernorm(x, axis=-1, eps=1e-05):
    m = jnp.mean(x, axis=axis, keepdims=True)
    v = jnp.var(x, axis=axis, keepdims=True)
    return (x - m) / jnp.sqrt(v + eps)

def _scatter_add(tgt, idx, src, axis=0):
    return tgt.at[idx].add(src)

def _segment_sum(src, seg, n):
    return jax.ops.segment_sum(src, seg, n)
kernel_name = 'mk_xattn_ffn_d2_seqx_r8_b511b6'

def setup_inputs(seed: int=0):
    np.random.seed(seed)
    _w = jnp.asarray

    def _rec_inputs():
        import jax
        import jax.numpy as jnp
        _rk = jax.random.key(seed)
        x = -0.0002928 + 1 * jax.random.normal(jax.random.fold_in(_rk, 1), (4, 256, 128), jnp.float32)
        _lenS = 256 - jax.random.randint(jax.random.fold_in(_rk, 7), (4,), 0, max(1, 256 // 4) + 1, jnp.int32)
        _lenS2 = 512 - jax.random.randint(jax.random.fold_in(_rk, 8), (4,), 0, max(1, 512 // 4) + 1, jnp.int32)
        _ctx_1024P = jax.random.normal(jax.random.fold_in(_rk, 11), (4, 16, 128), jnp.float32)
        _ctx_1024c = jax.random.dirichlet(jax.random.fold_in(_rk, 511), 0.3 * jnp.ones((16,), jnp.float32), (4, 512))
        _ctx_1024t = jnp.einsum('bsk,bkd->bsd', _ctx_1024c, _ctx_1024P)
        _ctx_1024t = _ctx_1024t * jax.lax.rsqrt(jnp.mean(jnp.square(_ctx_1024t)) + 1e-12) * 0.953939
        ctx_1024 = -1.39393e-06 + 0.999914 * (_ctx_1024t + 0.3 * jax.random.normal(jax.random.fold_in(_rk, 611), (4, 512, 128), jnp.float32))
        _validS = jnp.arange(256)[None, :] < _lenS[:, None]
        _validS2 = jnp.arange(512)[None, :] < _lenS2[:, None]
        _causal = jnp.tril(jnp.ones((256, 256), dtype=bool))
        mask_BxSxS2_bf1 = jnp.ones((4, 256, 512), dtype=bool)
        mask_Bx1xSxS2_ik1 = jnp.where(jnp.broadcast_to(_validS2[:, None, None, :], (4, 1, 256, 512)), 1, 0).astype(jnp.int32)
        return (x, ctx_1024, mask_BxSxS2_bf1, mask_Bx1xSxS2_ik1)
    x, ctx_1024, mask_BxSxS2_bf1, mask_Bx1xSxS2_ik1 = _rec_inputs()

    def _L0_xattn_setup():
        import jax, jax.numpy as jnp
        import numpy as np
        DIM = 128
        HEAD_DIM = 64
        NUM_HEADS = DIM // HEAD_DIM
        SCALE = HEAD_DIM ** (-0.5)
        key = jax.random.key(seed)
        k_x, k_ctx, k_wq, k_wkv, k_wo = jax.random.split(key, 5)
        B, N, M = (2, 256, 256)
        x = jax.random.normal(k_x, (B, N, DIM), dtype=jnp.float32)
        context = jax.random.normal(k_ctx, (B, M, DIM), dtype=jnp.float32)
        mask = jnp.ones((B, N, M), dtype=bool)
        s = DIM ** (-0.5)
        Wq = jax.random.normal(k_wq, (DIM, DIM), dtype=jnp.float32) * s
        Wkv = jax.random.normal(k_wkv, (DIM, 2 * DIM), dtype=jnp.float32) * s
        Wo = jax.random.normal(k_wo, (DIM, DIM), dtype=jnp.float32) * s
        return {'x': x, 'context': context, 'mask': mask, 'Wq': Wq, 'Wkv': Wkv, 'Wo': Wo}
    _L0_xattn_all = _L0_xattn_setup()
    _L0_xattn_in = {k: v for k, v in _L0_xattn_all.items() if k in ('Wq', 'Wkv', 'Wo')}
    del _L0_xattn_all

    def _L0_ffn_setup():
        import jax, jax.numpy as jnp
        import numpy as np
        DIM = 128

        def _reference_tuple_inner(x, W_r, W_k, W_v, mu_r, mu_k):
            B, T, C = x.shape
            x_prev = jnp.concatenate([jnp.zeros((B, 1, C), x.dtype), x[:, :-1, :]], axis=1)
            xr = mu_r * x + (1.0 - mu_r) * x_prev
            xk = mu_k * x + (1.0 - mu_k) * x_prev
            r = jax.nn.sigmoid(jnp.einsum('btc,dc->btd', xr, W_r))
            k = jnp.einsum('btc,dc->btd', xk, W_k)
            k_act = jnp.square(jax.nn.relu(k))
            out = r * jnp.einsum('btc,dc->btd', k_act, W_v)
            new_state = x[:, -1, :]
            return (out, new_state)
        key = jax.random.key(seed)
        ks = jax.random.split(key, 6)
        B, T, C = (8, 256, DIM)
        x = jax.random.normal(ks[0], (B, T, C), dtype=jnp.float32)
        s = 1.0 / np.sqrt(C)
        W_r = jax.random.uniform(ks[1], (C, C), jnp.float32, -s, s)
        W_k = jax.random.uniform(ks[2], (C, C), jnp.float32, -s, s)
        W_v = jax.random.uniform(ks[3], (C, C), jnp.float32, -s, s)
        mu_r = jax.random.uniform(ks[4], (C,), jnp.float32)
        mu_k = jax.random.uniform(ks[5], (C,), jnp.float32)
        return {'x': x, 'W_r': W_r, 'W_k': W_k, 'W_v': W_v, 'mu_r': mu_r, 'mu_k': mu_k}
    _L0_ffn_all = _L0_ffn_setup()
    _L0_ffn_in = {k: v for k, v in _L0_ffn_all.items() if k in ('W_r', 'W_k', 'W_v', 'mu_r', 'mu_k')}
    del _L0_ffn_all

    def _L1_xattn_setup():
        import jax, jax.numpy as jnp
        import numpy as np
        import math
        D_MODEL = 128
        NUM_HEADS = 16
        D_K = D_MODEL // NUM_HEADS
        B, S = (2, 256)

        def _split_heads(x):
            b, s, _ = x.shape
            return x.reshape(b, s, NUM_HEADS, D_K).transpose(0, 2, 1, 3)
        key = jax.random.key(seed)
        ks = jax.random.split(key, 13)
        scale = 1.0 / math.sqrt(D_MODEL)
        inp = {'q': jax.random.normal(ks[0], (B, S, D_MODEL), jnp.float32), 'k': jax.random.normal(ks[1], (B, S, D_MODEL), jnp.float32), 'v': jax.random.normal(ks[2], (B, S, D_MODEL), jnp.float32), 'mask': jax.random.randint(ks[3], (B, 1, S, S), 0, 2, jnp.int32), 'wQ_w': jax.random.normal(ks[4], (D_MODEL, D_MODEL), jnp.float32) * scale, 'wQ_b': jax.random.normal(ks[5], (D_MODEL,), jnp.float32) * scale, 'wK_w': jax.random.normal(ks[6], (D_MODEL, D_MODEL), jnp.float32) * scale, 'wK_b': jax.random.normal(ks[7], (D_MODEL,), jnp.float32) * scale, 'wV_w': jax.random.normal(ks[8], (D_MODEL, D_MODEL), jnp.float32) * scale, 'wV_b': jax.random.normal(ks[9], (D_MODEL,), jnp.float32) * scale, 'wO_w': jax.random.normal(ks[10], (D_MODEL, D_MODEL), jnp.float32) * scale, 'wO_b': jax.random.normal(ks[11], (D_MODEL,), jnp.float32) * scale}
        return inp
    _L1_xattn_all = _L1_xattn_setup()
    _L1_xattn_in = {k: v for k, v in _L1_xattn_all.items() if k in ('wQ_w', 'wQ_b', 'wK_w', 'wK_b', 'wV_w', 'wV_b', 'wO_w', 'wO_b')}
    del _L1_xattn_all

    def _L1_ffn_setup():
        import jax, jax.numpy as jnp
        import numpy as np
        S, B, H, I, E = (64, 2, 128, 352, 8)
        key = jax.random.key(seed)
        ks = jax.random.split(key, 5)
        return {'hidden_states': jax.random.normal(ks[0], (S, B, H), dtype=jnp.float32), 'router_w': jax.random.normal(ks[1], (E, H), dtype=jnp.float32) * 0.02, 'gate_w': jax.random.normal(ks[2], (E, I, H), dtype=jnp.float32) * 0.02, 'up_w': jax.random.normal(ks[3], (E, I, H), dtype=jnp.float32) * 0.02, 'down_w': jax.random.normal(ks[4], (E, H, I), dtype=jnp.float32) * 0.02}
    _L1_ffn_all = _L1_ffn_setup()
    _L1_ffn_in = {k: v for k, v in _L1_ffn_all.items() if k in ('router_w', 'gate_w', 'up_w', 'down_w')}
    del _L1_ffn_all
    return {'x': x, 'ctx_1024': ctx_1024, 'mask_BxSxS2_bf1': mask_BxSxS2_bf1, 'mask_Bx1xSxS2_ik1': mask_Bx1xSxS2_ik1, 'L0_xattn_Wq': _L0_xattn_in['Wq'], 'L0_xattn_Wkv': _L0_xattn_in['Wkv'], 'L0_xattn_Wo': _L0_xattn_in['Wo'], 'L0_ffn_W_r': _L0_ffn_in['W_r'], 'L0_ffn_W_k': _L0_ffn_in['W_k'], 'L0_ffn_W_v': _L0_ffn_in['W_v'], 'L0_ffn_mu_r': _L0_ffn_in['mu_r'], 'L0_ffn_mu_k': _L0_ffn_in['mu_k'], 'L1_xattn_wQ_w': _L1_xattn_in['wQ_w'], 'L1_xattn_wQ_b': _L1_xattn_in['wQ_b'], 'L1_xattn_wK_w': _L1_xattn_in['wK_w'], 'L1_xattn_wK_b': _L1_xattn_in['wK_b'], 'L1_xattn_wV_w': _L1_xattn_in['wV_w'], 'L1_xattn_wV_b': _L1_xattn_in['wV_b'], 'L1_xattn_wO_w': _L1_xattn_in['wO_w'], 'L1_xattn_wO_b': _L1_xattn_in['wO_b'], 'L1_ffn_router_w': _L1_ffn_in['router_w'], 'L1_ffn_gate_w': _L1_ffn_in['gate_w'], 'L1_ffn_up_w': _L1_ffn_in['up_w'], 'L1_ffn_down_w': _L1_ffn_in['down_w']}

def reference(x, ctx_1024, mask_BxSxS2_bf1, mask_Bx1xSxS2_ik1, L0_xattn_Wq, L0_xattn_Wkv, L0_xattn_Wo, L0_ffn_W_r, L0_ffn_W_k, L0_ffn_W_v, L0_ffn_mu_r, L0_ffn_mu_k, L1_xattn_wQ_w, L1_xattn_wQ_b, L1_xattn_wK_w, L1_xattn_wK_b, L1_xattn_wV_w, L1_xattn_wV_b, L1_xattn_wO_w, L1_xattn_wO_b, L1_ffn_router_w, L1_ffn_gate_w, L1_ffn_up_w, L1_ffn_down_w):
    import jax
    import jax.numpy as jnp

    def _L0_xattn_ref(x, context, mask, Wq, Wkv, Wo):
        import jax, jax.numpy as jnp
        import numpy as np
        DIM = 128
        HEAD_DIM = 64
        NUM_HEADS = DIM // HEAD_DIM
        SCALE = HEAD_DIM ** (-0.5)
        B, N, C = x.shape
        M = context.shape[1]
        H, D = (NUM_HEADS, HEAD_DIM)
        q = (x @ Wq).reshape(B, N, H, D).transpose(0, 2, 1, 3)
        kv = (context @ Wkv).reshape(B, M, 2, H, D).transpose(2, 0, 3, 1, 4)
        k, v = (kv[0], kv[1])
        attn = jnp.einsum('bhnd,bhmd->bhnm', q, k) * SCALE
        attn = jnp.where(mask[:, None, :, :], attn, -jnp.inf)
        attn = jax.nn.softmax(attn, axis=-1)
        out = jnp.einsum('bhnm,bhmd->bhnd', attn, v)
        out = out.transpose(0, 2, 1, 3).reshape(B, N, C)
        return out @ Wo

    def _L0_ffn_ref(x, W_r, W_k, W_v, mu_r, mu_k):
        import jax, jax.numpy as jnp
        import numpy as np
        DIM = 128

        def _reference_tuple_inner(x, W_r, W_k, W_v, mu_r, mu_k):
            B, T, C = x.shape
            x_prev = jnp.concatenate([jnp.zeros((B, 1, C), x.dtype), x[:, :-1, :]], axis=1)
            xr = mu_r * x + (1.0 - mu_r) * x_prev
            xk = mu_k * x + (1.0 - mu_k) * x_prev
            r = jax.nn.sigmoid(jnp.einsum('btc,dc->btd', xr, W_r))
            k = jnp.einsum('btc,dc->btd', xk, W_k)
            k_act = jnp.square(jax.nn.relu(k))
            out = r * jnp.einsum('btc,dc->btd', k_act, W_v)
            new_state = x[:, -1, :]
            return (out, new_state)
        return _reference_tuple_inner(x, W_r, W_k, W_v, mu_r, mu_k)[0]

    def _L1_xattn_ref(q, k, v, mask, wQ_w, wQ_b, wK_w, wK_b, wV_w, wV_b, wO_w, wO_b):
        import jax, jax.numpy as jnp
        import numpy as np
        import math
        D_MODEL = 128
        NUM_HEADS = 16
        D_K = D_MODEL // NUM_HEADS
        B, S = (2, 256)

        def _split_heads(x):
            b, s, _ = x.shape
            return x.reshape(b, s, NUM_HEADS, D_K).transpose(0, 2, 1, 3)
        qh = _split_heads(q @ wQ_w.T + wQ_b)
        kh = _split_heads(k @ wK_w.T + wK_b)
        vh = _split_heads(v @ wV_w.T + wV_b)
        scores = jnp.einsum('bhsd,bhtd->bhst', qh, kh) / math.sqrt(D_K)
        scores = jnp.where(mask == 0, jnp.float32(-1000000000.0), scores)
        attn = jax.nn.softmax(scores, axis=-1)
        out = jnp.einsum('bhst,bhtd->bhsd', attn, vh)
        out = out.transpose(0, 2, 1, 3).reshape(q.shape[0], -1, D_MODEL)
        return out @ wO_w.T + wO_b

    def _L1_ffn_ref(hidden_states, router_w, gate_w, up_w, down_w):
        import jax, jax.numpy as jnp
        import numpy as np
        S, B, H, I, E = (64, 2, 128, 352, 8)
        router_logits = jnp.einsum('sbh,eh->sbe', hidden_states, router_w)
        routing_indices = jnp.argmax(router_logits, axis=-1)
        out = jnp.zeros_like(hidden_states)
        for e in range(E):
            mask = (routing_indices == e)[..., None]
            xe = jnp.where(mask, hidden_states, 0.0)
            g = jnp.einsum('sbh,ih->sbi', xe, gate_w[e])
            u = jnp.einsum('sbh,ih->sbi', xe, up_w[e])
            ye = jnp.einsum('sbi,hi->sbh', jax.nn.silu(g) * u, down_w[e])
            out = out + jnp.where(mask, ye, 0.0)
        return out
    x = x + _L0_xattn_ref(_layernorm(x, axis=-1), ctx_1024, mask_BxSxS2_bf1, L0_xattn_Wq, L0_xattn_Wkv, L0_xattn_Wo)
    x = x + _L0_ffn_ref(_layernorm(x, axis=-1), L0_ffn_W_r, L0_ffn_W_k, L0_ffn_W_v, L0_ffn_mu_r, L0_ffn_mu_k)
    x = x + _L1_xattn_ref(_layernorm(x, axis=-1), ctx_1024, ctx_1024, mask_Bx1xSxS2_ik1, L1_xattn_wQ_w, L1_xattn_wQ_b, L1_xattn_wK_w, L1_xattn_wK_b, L1_xattn_wV_w, L1_xattn_wV_b, L1_xattn_wO_w, L1_xattn_wO_b)
    x = x + _L1_ffn_ref(_layernorm(x, axis=-1), L1_ffn_router_w, L1_ffn_gate_w, L1_ffn_up_w, L1_ffn_down_w)
    return x

_drawn_inputs = setup_inputs


def setup_inputs(seed=0):
    import zlib

    import numpy as np

    out = dict(_drawn_inputs(seed))
    spreads = {}
    factors = {'L0_ffn_W_r': 3.493,
     'L0_ffn_mu_r': 7.997,
     'L1_xattn_wQ_b': 3.136,
     'L1_xattn_wK_b': 8.0,
     'L1_ffn_router_w': 7.82,
     'L1_ffn_gate_w': 7.367,
     'L1_ffn_up_w': 7.352,
     'L1_ffn_down_w': 7.365}
    for name, (base, spread) in spreads.items():
        noise = np.random.default_rng([zlib.crc32(name.encode()), seed]).standard_normal(out[name].shape)
        drawn = base * np.exp(spread * noise) if base else spread * noise
        out[name] = jnp.asarray(drawn.astype(out[name].dtype))
    for name, factor in factors.items():
        out[name] = (out[name] * factor).astype(out[name].dtype)
    return out
```

```python
import concourse.bass as bass
from concourse import mybir
from contextlib import ExitStack

F32 = mybir.dt.float32
BF16 = mybir.dt.bfloat16
I32 = mybir.dt.int32
U32 = mybir.dt.uint32
ALU = mybir.AluOpType
ACT = mybir.ActivationFunctionType
AX_X = mybir.AxisListType.X

P = 128
B, SQ, SK, D = 4, 256, 512, 128
QT, KT = SQ // P, SK // P
TILES = B * QT
TOK = B * SQ
H0, D0 = 2, 64
H1, D1 = 16, 8
SPLIT = 3
ROWS = SPLIT * SPLIT * D1
GH = 4
GROUPS = H1 // GH
UNITS = B * GROUPS
MROWS = 2 * GH
E, I = 8, 352
ITILES = [(0, 128), (128, 128), (256, 96)]
SLOT_TILES = (TOK - E) // P + E
BIG = float(2 ** 32)
EPS = 1e-5
VW = 32

W_SIZES = [("Wq0", 128), ("Wk0", 128), ("Wv0", 128), ("Wo0", 128), ("Wr", 128), ("Wk", 128), ("Wv", 128),
           ("wQ", 128), ("wK", 128), ("wV", 128), ("wO", 128), ("router", E), ("mu_r", 1), ("mu_k", 1),
           ("bQ", 1), ("bK", 1), ("bV", 128), ("bO", 128)]
C_SIZES = [("ident", 128), ("tri", 128), ("rank8", 64), ("floor8", 64), ("thresholds", 64), ("before", 64),
           ("slot_tile", SLOT_TILES * E)]


def columns(sizes):
    at, out = 0, {}
    for name, n in sizes:
        out[name] = (at, at + n)
        at += n
    return out, at


WCOL, WTOT = columns(W_SIZES)
CCOL, CTOT = columns(C_SIZES)


def first_jobs():
    jobs = ["lnT0", "lnT1", "q0", "q1"] + [f"k0_{b}" for b in range(B)] + [f"v0_{b}" for b in range(B)]
    n = B * H0 * QT
    jobs += ["S0", "S1"]
    for u in range(n + 2):
        if u + 2 < n:
            jobs.append(f"S{u + 2}")
        if 1 <= u <= n:
            jobs.append(f"T{u - 1}")
        if u >= 5 and (u - 5) % 4 == 0:
            jobs.append(f"PV{(u - 5) // 4}")
        if u % 4 == 1 and u < n:
            jobs += [f"K{u // 4}", f"V{u // 4}"]
    jobs += ["F0", "F1"]
    for name in ("wo", "l2T", "kk", "rr", "vv", "l3T", "Q"):
        jobs += [f"{name}0", f"{name}1"]
    return jobs


JOBS = {name: n for n, name in enumerate(first_jobs())}


def last_jobs():
    return ["oT0", "oT1", "wo0", "wo1", "nT0", "nT1", "lg", "pos", "cnt"]


JOBS2 = {name: n for n, name in enumerate(last_jobs())}


def build(nc, x_d, ctxT_d, m0_d, m1_d, m1k_d, w_d, gu_d, dn_d, c_d, sel_d, out_d):
    scrK = nc.dram_tensor("k_parts_dram", (SPLIT, SPLIT, P, B * SK), BF16, kind="Internal").ap()
    scrQ = nc.dram_tensor("q_parts_dram", (SPLIT, SPLIT, P, B * SQ), BF16, kind="Internal").ap()
    xs_d = nc.dram_tensor("sorted_in_dram", (SLOT_TILES * P, D), F32, kind="Internal").ap()
    ys_d = nc.dram_tensor("sorted_out_dram", (SLOT_TILES * P, D), F32, kind="Internal").ap()

    with ExitStack() as ctx:
        def sb(name, shape, dt=F32):
            return ctx.enter_context(nc.sbuf_tensor(name, shape, dt))[:]

        def sem(name):
            return ctx.enter_context(nc.semaphore(name))

        ps = ctx.enter_context(nc.psum_tensor("banks", [P, 8, 512], F32))[:]

        k_raw = sb("k_region", [P, 16384])
        q_raw = sb("q_region", [P, 8192])
        p_raw = sb("p_region", [P, 8192])
        c_raw = sb("ctx_region", [P, 2048])
        m0b = sb("mask0_bias", [P, TILES * SK], BF16)
        m1b = sb("mask1_bias", [P, TILES, SK], BF16)
        m1kb = sb("mask1_bias_by_key", [P, B * KT, SQ], BF16)
        v1 = sb("values1", [P, B * KT, D])
        vst = sb("values_staged", [P, 2, KT, GH, VW])
        junk = sb("scores_unused", [P, 2, SK], BF16)
        x = sb("x", [P, TILES, D])
        ln = sb("normed", [P, TILES, D])
        lnT = sb("normed_T", [P, TOK])
        w = sb("weights", [P, WTOT])
        cst = sb("constants", [P, CTOT])
        identB = sb("ident_bf", [P, P], BF16)
        onesB = sb("ones_bf", [P, P], BF16)
        triB = sb("tri_bf", [P, P], BF16)
        part32 = sb("split_rest", [P, 2, 512])
        parts = sb("split_parts", [P, 2, SPLIT, 512], BF16)
        stats = sb("ln_stats", [P, TILES, 6])
        mv = sb("ln_mean_var", [P, TILES, 2])
        rstd = sb("ln_rstd", [P, TILES])
        veps = sb("ln_var_eps", [P, TILES])
        mhalf = sb("minus_half", [P, TILES])
        omu = sb("one_minus_mu", [P, 2])
        mx0 = sb("max0", [P, 16])
        nm0 = sb("neg_max0", [P, 16])
        den0 = sb("sum0", [P, 16])
        rd0 = sb("inv_sum0", [P, 16])
        anym = sb("any_key", [P, 2, TILES])
        mx1 = sb("max1", [P, 2, QT, GH])
        nm1 = sb("neg_max1_parts", [P, 2, QT, 2, GH], BF16)
        rden = sb("inv_sum1", [P, 2, QT, GH])

        def W(name):
            return w[:, WCOL[name][0]:WCOL[name][1]]

        def C(name):
            return cst[:, CCOL[name][0]:CCOL[name][1]]

        ident = C("ident")
        kst = k_raw.bitcast(BF16)
        qst = q_raw.bitcast(BF16)
        k0T = q_raw[:, 0:2048]
        v0 = q_raw[:, 2048:4096].rearrange("p (t c) -> p t c", t=B * KT)
        pr0 = q_raw[:, 4096:6144].rearrange("p (r k) -> p r k", r=4)
        q0T = q_raw[:, 6144:7168]
        m0u = q_raw[:, 7168:8192].bitcast(m0_d.dtype)
        m1i = p_raw[:, 0:4096].bitcast(I32).rearrange("p (t k) -> p t k", t=TILES)
        m1ki = p_raw[:, 4096:8192].bitcast(I32).rearrange("p (t k) -> p t k", t=B * KT)
        pt0 = p_raw[:, 0:4096].rearrange("p (r h t q) -> p r h t q", r=2, h=H0, t=KT)
        ln2T = p_raw[:, 4096:4096 + B * 257].rearrange("p (b q) -> p b q", b=B)
        xkT = p_raw[:, 5124:6148]
        xrT = p_raw[:, 6148:7172]
        prv = p_raw[:, 7172:7684].rearrange("p (b q) -> p b q", b=2)
        prv2 = p_raw[:, 7684:8192]
        kact = c_raw[:, 0:1024]
        sig = c_raw[:, 1024:2048].rearrange("p (t c) -> p t c", t=TILES)
        fq = m0b.bitcast(F32)[:, 0:1024]
        ln3T = m0b.bitcast(F32)[:, 1024:2048]
        diag = p_raw[:, 0:512].bitcast(BF16).rearrange("p (t c) -> p t c", t=TILES)
        pt = p_raw.rearrange("p (r j t q) -> p r j t q", r=2, j=GH, t=KT)
        otok = c_raw[:, 0:1024].rearrange("p (t c) -> p t c", t=TILES)
        osb = c_raw[:, 1024:1536].rearrange("p (r q) -> p r q", r=2)
        zeros = c_raw[:, 1536:1664]
        gu = k_raw[:, 0:5632]
        dn = k_raw[:, 5632:8704].rearrange("p (i n) -> p i n", i=3)
        gin = k_raw[:, 8704:8704 + SLOT_TILES * D].rearrange("p (s c) -> p s c", s=SLOT_TILES)
        n3T = q_raw[:, 0:1024]
        ginT = q_raw[:, 1024:1280].rearrange("p (r q) -> p r q", r=2)
        hT = q_raw[:, 1280:2048].rearrange("p (r q) -> p r q", r=2)
        eg = q_raw[:, 2048:2752].rearrange("p (r q) -> p r q", r=2)
        hh = q_raw[:, 2752:3456].rearrange("p (r q) -> p r q", r=2)
        yo = q_raw[:, 3456:3712].rearrange("p (r q) -> p r q", r=2)
        yg = q_raw[:, 4096:5120].rearrange("p (t c) -> p t c", t=TILES)
        rt = q_raw[:, 5120:6144]
        o1T = p_raw[:, 0:1024]
        m1s = lnT.bitcast(BF16).rearrange("p (r q k) -> p r q k", r=2, q=QT)
        slot_u = rt[:, 640:648].bitcast(U32)
        experts = rt[0:1, 704:704 + SLOT_TILES].bitcast(I32)

        x_in, w_in, c_in = sem("x_in"), sem("w_in"), sem("c_in")
        ctx_in = [sem(f"ctx_in{b}") for b in range(B)]
        m0_in, m1_in, m1k_in = sem("m0_in"), sem("m1_in"), sem("m1k_in")
        full = [sem(f"bank_full{k}") for k in range(8)]
        free = [sem(f"bank_free{k}") for k in range(8)]
        full2 = [sem(f"bank2_full{k}") for k in range(8)]
        free2 = [sem(f"bank2_free{k}") for k in range(8)]
        const_bf = sem("const_bf")
        ln_done = sem("ln_done")
        dve_step = sem("dve_step")
        half_set, var_ready, rstd_ready = sem("half_set"), sem("var_ready"), sem("rstd_ready")
        m0_conv, m1_conv, m1k_conv = sem("m0_conv"), sem("m1_conv"), sem("m1k_conv")
        negmax0, exp0, inv0, probs0 = sem("negmax0"), sem("exp0"), sem("inv0"), sem("probs0")
        k_split, k_wr, q_split, q_wr = sem("k_split"), sem("k_wr"), sem("q_split"), sem("q_wr")
        k_in = [sem(f"k_in{b}") for b in range(B)]
        q_in = [sem(f"q_in{h}") for h in range(2)]
        sel_in = sem("sel_in")
        diag_done = sem("diag_done")
        xr_done, xk_done, kact_done = sem("xr_done"), sem("xk_done"), sem("kact_done")
        q_rows0, xb_done = sem("q_rows0"), sem("xb_done")
        vst_ones = sem("vst_ones")
        nm_hi, rd_done = sem("neg_max1_high"), sem("inv_sum1_done")
        sq_ready, sq_used = sem("score_q_ready"), sem("score_q_used")
        negmax1, mt_ready, mrows = sem("negmax1"), sem("mt_ready"), sem("mrows_ready")
        st_ready, exp1 = sem("score_k_ready"), sem("exp1")
        m1s_done = sem("m1s_done")
        vst_done, pv_done, oevac = sem("vst_done"), sem("pv_done"), sem("o_copied")
        ot_ready, otok_done = sem("ot_ready"), sem("otok_done")
        moe_w_in, zero_set, xs_zero = sem("moe_w_in"), sem("zero_set"), sem("xs_zero")
        o1T_done, n3T_done, lnC_done = sem("o1T_done"), sem("n3T_done"), sem("lnC_done")
        onehot_done, slot_done, experts_done = sem("onehot_done"), sem("slot_done"), sem("experts_done")
        scattered, gin_in = sem("scattered"), sem("gin_in")
        gT_ready, gT_copied = sem("gT_ready"), sem("gT_copied")
        gu_ready, eg_done, silu_done, h_done = sem("gu_ready"), sem("eg_done"), sem("silu_done"), sem("h_done")
        hT_ready, hT_copied, y_ready, y_copied = sem("hT_ready"), sem("hT_copied"), sem("y_ready"), sem("y_copied")
        ys_out = [sem("ys_out_even"), sem("ys_out_odd")]
        yg_in, fin_done, out_done = sem("yg_in"), sem("fin_done"), sem("out_done")

        block = ctx.enter_context(nc.Block())

        def bank(job, jobs=JOBS):
            return ps[:, jobs[job] % 8, :]

        def claim(eng, job, jobs=JOBS, sems=None):
            n = jobs[job]
            if n >= 8:
                eng.wait_ge((sems or free)[n % 8], n // 8)

        def arrived(eng, job, jobs=JOBS, sems=None):
            n = jobs[job]
            eng.wait_ge((sems or full)[n % 8], n // 8 + 1)

        def filled(ins, job):
            ins.then_inc(full[JOBS[job] % 8], 1)

        def emptied(ins, job):
            ins.then_inc(free[JOBS[job] % 8], 1)

        def copied(eng, job):
            n = JOBS[job]
            eng.wait_ge(free[n % 8], n // 8 + 1)

        def counted(ns, of, i, value, count):
            if isinstance(i, int):
                ns.wait_ge(of, value)
            else:
                ns.wait_ge(of, ns.snap(count))
                ns.reg_add(count, count, 1)

        def pipeline(step):
            for s in range(-2, SLOT_TILES + 1):
                step(s, s % 2, lambda w: 0 <= w < SLOT_TILES)

        def unit(i, k):
            return 4 * i + k, i + k // 4, k % 4

        @block.sync
        def _(sp):
            sp.dma_start(x, x_d.rearrange("(t p) c -> p t c", p=P)).then_inc(x_in, 16)
            sp.dma_start(cst, c_d).then_inc(c_in, 16)
            sp.dma_start(w, w_d).then_inc(w_in, 16)
            for b in range(B):
                sp.dma_start(c_raw[:, b * SK:(b + 1) * SK], ctxT_d[:, b * SK:(b + 1) * SK]).then_inc(ctx_in[b], 16)
            sp.dma_start(k_raw[0:MROWS, :].rearrange("p (u n) -> p u n", u=UNITS),
                         sel_d.unsqueeze(1).broadcast_to([MROWS, UNITS, GH * SK // 2])).then_inc(sel_in, 16)
            for b in range(B):
                sp.wait_ge(k_split, b + 1)
                for i in range(SPLIT):
                    sp.dma_start(scrK[i, :, :, b * SK:(b + 1) * SK].rearrange("j p n -> p j n"),
                                 parts[:, b % 2, :, :]).then_inc(k_wr, 16)
                sp.wait_ge(k_wr, 16 * SPLIT * (b + 1))
                sp.dma_start(kst[MROWS:MROWS + ROWS, b * H1 * SK:(b + 1) * H1 * SK],
                             scrK.rearrange("i j (d h) n -> (i j d) h n", h=H1)[:, :, b * SK:(b + 1) * SK])\
                    .then_inc(k_in[b], 16)
            for h in range(2):
                sp.wait_ge(q_split, h + 1)
                for j in range(SPLIT):
                    sp.dma_start(scrQ[:, j, :, h * 512:(h + 1) * 512].rearrange("i p n -> p i n"),
                                 parts[:, h, :, :]).then_inc(q_wr, 16)
                sp.wait_ge(q_wr, 16 * SPLIT * (h + 1))
                for b in (2 * h, 2 * h + 1):
                    sp.dma_start(qst[MROWS:MROWS + ROWS, b * H1 * SQ:(b + 1) * H1 * SQ],
                                 scrQ.rearrange("i j (d h) n -> (i j d) h n", h=H1)[:, :, b * SQ:(b + 1) * SQ])\
                        .then_inc(q_in[h], 16)
            sp.wait_ge(zero_set, 1)
            sp.dma_start(xs_d.rearrange("(s p) c -> p s c", p=P),
                         zeros.unsqueeze(1).broadcast_to([P, SLOT_TILES, D])).then_inc(xs_zero, 16)
            sp.wait_ge(pv_done, 3 * GROUPS)
            sp.dma_start(gu, gu_d).then_inc(moe_w_in, 16)
            for n, (at, rows) in enumerate(ITILES):
                sp.dma_start(dn[0:rows, n, :], dn_d[at:at + rows, :]).then_inc(moe_w_in, 16)
            sp.wait_ge(scattered, 16 * TILES)
            sp.dma_start(gin, xs_d.rearrange("(s p) c -> p s c", p=P)).then_inc(gin_in, 16)
            def results_out(s, r):
                sp.wait_ge(y_copied, s + 1)
                sp.dma_start(ys_d[bass.ds(s * P, P), :], yo[:, r, :]).then_inc(ys_out[r], 16)

            with sp.Fori(0, SLOT_TILES // 2) as i:
                for r in range(2):
                    results_out(2 * i + r, r)
            results_out(SLOT_TILES - 1, (SLOT_TILES - 1) % 2)
            sp.wait_ge(fin_done, 1)
            sp.dma_start(out_d.rearrange("(t p) c -> p t c", p=P), x).then_inc(out_done, 16)
            sp.wait_ge(out_done, 16)

        @block.gpsimd
        def _(pool):
            g = nc.gpsimd
            norms = [0]

            def inverse_root(t0, t1):
                norms[0] += 1
                pool.wait_ge(var_ready, norms[0])
                g.tensor_tensor(rstd[:, t0:t1], veps[:, t0:t1], mhalf[:, t0:t1], ALU.pow).then_inc(rstd_ready, 1)

            g.memset(mhalf, -0.5).then_inc(half_set, 1)
            pool.wait_ge(half_set, 1)
            inverse_root(0, TILES)
            g.memset(vst, 1.0).then_inc(vst_ones, 1)
            g.memset(onesB, 1.0).then_inc(const_bf, 1)
            pool.wait_ge(c_in, 16)
            g.tensor_copy(identB, ident).then_inc(const_bf, 1)
            g.tensor_copy(triB, C("tri")).then_inc(const_bf, 1)
            pool.wait_ge(m0_in, 16)
            for b in range(B):
                c = slice(b * 1024, (b + 1) * 1024)
                g.tensor_scalar(m0b[:, c], m0u[:, c], 1.0, 3.4e38, ALU.subtract, ALU.mult).then_inc(m0_conv, 1)
            n = B * H0 * QT
            for u in range(n):
                pool.wait_ge(inv0, u + 1)
                g.tensor_scalar(pr0[:, u % 4, :], pr0[:, u % 4, :], rd0[:, u:u + 1], None, ALU.mult).then_inc(probs0, 1)
            for h in range(2):
                inverse_root(4 * h, 4 * h + 4)
            for h in range(2):
                copied(pool, f"kk{h}")
                c = slice(h * 512, (h + 1) * 512)
                g.tensor_tensor(kact[:, c], kact[:, c], kact[:, c], ALU.mult).then_inc(kact_done, 1)
            arrived(pool, "wo1")
            g.memset(q_raw[0:MROWS, :], 0.0).then_inc(q_rows0, 1)
            for h in range(2):
                inverse_root(4 * h, 4 * h + 4)
            pool.wait_ge(ln_done, 6)
            g.tensor_tensor(x, x, W("bO").unsqueeze(1).broadcast_to([P, TILES, D]), ALU.add).then_inc(xb_done, 1)
            g.memset(zeros, 0.0).then_inc(zero_set, 1)
            copied(pool, f"V{B - 1}")
            pool.wait_ge(vst_ones, 1)

            values_used, masks_used = g.alloc_register("values_used"), g.alloc_register("masks_used")

            def stage_values(i, k, par):
                u, b, grp = unit(i, k)
                if not (isinstance(i, int) and u < 2):
                    counted(g, pv_done, i, u - 1, values_used)
                src = v1[:, bass.ds(b * KT, KT), grp * 32:(grp + 1) * 32].rearrange("p t (j d) -> p t j d", j=GH)
                g.tensor_copy(vst[:, par, :, :, 0:D1], src).then_inc(vst_done, 1)

            def stage_mask(i, k, par):
                u, b, _ = unit(i, k)
                if not (isinstance(i, int) and u < 2):
                    counted(g, negmax1, i, u - 1, masks_used)
                src = m1b.rearrange("p t k -> p (t k)").bitcast(F32)[:, bass.ds(b * (QT * SK // 2), QT * SK // 2)]
                g.tensor_copy(m1s[:, par].rearrange("p q k -> p (q k)").bitcast(F32), src).then_inc(m1s_done, 1)

            arrived(pool, "wo1")
            stage_mask(0, 0, 0)
            stage_mask(0, 1, 1)
            for k in range(2):
                stage_mask(0, k + 2, k)
                stage_values(0, k, k)
            g.reg_mov(values_used, 1)
            g.reg_mov(masks_used, 3)
            with g.Fori(0, B - 1) as i:
                for k in range(2, 6):
                    stage_mask(i, k + 2, k % 2)
                    stage_values(i, k, k % 2)
            for k in range(2, 4):
                stage_values(B - 1, k, k % 2)
            for h in range(2):
                inverse_root(4 * h, 4 * h + 4)
            pool.wait_ge(xs_zero, 16)
            pool.wait_ge(slot_done, 1)
            pool.wait_ge(lnC_done, 2)
            for t in range(TILES):
                g.indirect_dma_start(xs_d, bass.IndirectOffsetOnAxis(ap=slot_u[:, t:t + 1], axis=0),
                                     ln[:, t, :], None).then_inc(scattered, 16)
            pool.wait_ge(ys_out[0], 16 * ((SLOT_TILES + 1) // 2))
            pool.wait_ge(ys_out[1], 16 * (SLOT_TILES // 2))
            for t in range(TILES):
                g.indirect_dma_start(yg[:, t, :], None, ys_d,
                                     bass.IndirectOffsetOnAxis(ap=slot_u[:, t:t + 1], axis=0)).then_inc(yg_in, 16)

        @block.scalar
        def _(act):
            a = nc.scalar
            act.dma_start(m0u, m0_d).then_inc(m0_in, 16)
            act.dma_start(m1i, m1_d).then_inc(m1_in, 16)
            act.dma_start(m1ki, m1k_d).then_inc(m1k_in, 16)
            for h in range(2):
                arrived(act, f"lnT{h}")
                emptied(a.activation(lnT[:, h * 512:(h + 1) * 512], bank(f"lnT{h}"), ACT.Copy), f"lnT{h}")
            for h in range(2):
                arrived(act, f"q{h}")
                if h == 0:
                    act.wait_ge(m0_in, 16)
                emptied(a.activation(q0T[:, h * 512:(h + 1) * 512], bank(f"q{h}"), ACT.Copy), f"q{h}")
            for b in range(B):
                arrived(act, f"v0_{b}")
                emptied(a.activation(v0[:, b * KT:(b + 1) * KT, :], bank(f"v0_{b}").rearrange("p (t c) -> p t c", t=KT),
                                     ACT.Copy), f"v0_{b}")
            n = B * H0 * QT
            for u in range(n + 2):
                if u < n:
                    act.wait_ge(negmax0, u + 1)
                    a.activation(pr0[:, u % 4, :], pr0[:, u % 4, :], ACT.Exp, bias=nm0[:, u:u + 1], scale=float(D0) ** -0.5,
                                 accum_out=den0[:, u:u + 1]).then_inc(exp0, 1)
                v = u - 1
                if 0 <= v < n and v % 2 == 0:
                    b, h, q = v // 4, v // 2 % 2, v % 2
                    arrived(act, f"T{v}")
                    if v == 0:
                        act.wait_ge(m1_conv, 1)
                    if b >= 2:
                        arrived(act, f"PV{b - 2}")
                    emptied(a.activation(pt0[:, b % 2, h, :, q * P:(q + 1) * P], bank(f"T{v}").rearrange("p (t q) -> p t q", t=KT),
                                         ACT.Copy), f"T{v}")
                if u >= 5 and (u - 5) % 4 == 0:
                    b = (u - 5) // 4
                    arrived(act, f"PV{b}")
                    emptied(a.activation(lnT[:, b * SQ:(b + 1) * SQ], bank(f"PV{b}")[:, 0:SQ], ACT.Copy), f"PV{b}")
            for h in range(2):
                act.wait_ge(negmax0, n)
                arrived(act, f"F{h}")
                emptied(a.activation(fq[:, h * 512:(h + 1) * 512], bank(f"F{h}"), ACT.Copy), f"F{h}")
            act.wait_ge(m1k_conv, 1)
            for h in range(2):
                arrived(act, f"l2T{h}")
                emptied(a.activation(ln2T[:, 2 * h:2 * h + 2, 1:257], bank(f"l2T{h}").rearrange("p (b q) -> p b q", b=2),
                                     ACT.Copy), f"l2T{h}")
            for h in range(2):
                arrived(act, f"kk{h}")
                if h == 0:
                    arrived(act, f"V{B - 1}")
                emptied(a.activation(kact[:, h * 512:(h + 1) * 512], bank(f"kk{h}"), ACT.Relu), f"kk{h}")
            for h in range(2):
                arrived(act, f"rr{h}")
                emptied(a.activation(sig[:, 4 * h:4 * h + 4, :], bank(f"rr{h}").rearrange("p (t c) -> p t c", t=4), ACT.Exp,
                                     scale=-1.0), f"rr{h}")
            for h in range(2):
                arrived(act, f"l3T{h}")
                emptied(a.activation(ln3T[:, h * 512:(h + 1) * 512], bank(f"l3T{h}"), ACT.Copy), f"l3T{h}")

            def minus_max_rows(i, k, par):
                u, _, _ = unit(i, k)
                act.wait_ge(mt_ready, u + 1)
                src = ps[:, 6 + (par ^ 1), 256:384].bitcast(BF16)[0:MROWS, :]
                dst = qst[0:MROWS, bass.ds(u * (GH * SQ), GH * SQ)].rearrange("p (j q) -> p j q", j=GH)
                a.activation(dst, src.unsqueeze(1).broadcast_to([MROWS, GH, SQ]), ACT.Copy).then_inc(mrows, 1)

            def copy_out(i, k, par):
                u, _, _ = unit(i, k)
                act.wait_ge(pv_done, u + 1)
                if not (isinstance(i, int) and u < 2):
                    act.wait_ge(ot_ready, u - 1)
                a.activation(osb[:, par, :], ps[:, 6 + par, 0:SQ], ACT.Copy).then_inc(oevac, 1)

            def exps(i, k, par, heads):
                u, _, _ = unit(i, k)
                for j in heads:
                    n = 4 * u + j
                    act.wait_ge(st_ready, n + 1)
                    if j == 0 and not (isinstance(i, int) and u < 2):
                        act.wait_ge(pv_done, u - 1)
                    c = 2 * (j % 2)
                    a.activation(pt[:, par, j, :, :].rearrange("p (c t) q -> p c (t q)", c=2), ps[:, c:c + 2, :],
                                 ACT.Exp, scale=float(D1) ** -0.5).then_inc(exp1, 1)

            act.wait_ge(ln_done, 6)
            arrived(act, "Q1")
            act.wait_ge(q_rows0, 1)
            minus_max_rows(0, 0, 0)

            def body(i, k, peel_front=0, more=True):
                par = k % 2
                if peel_front >= 2:
                    copy_out(i, k - 2, par)
                exps(i, k, par, (0,))
                if more:
                    minus_max_rows(i, k + 1, par ^ 1)
                exps(i, k, par, (1, 2, 3))

            body(0, 0, 0)
            body(0, 1, 0)
            body(0, 2, 2)
            body(0, 3, 2)
            with a.Fori(0, B - 2) as i:
                for k in range(4, 8):
                    body(i, k, 2)
            for k in range(4, 8):
                body(B - 2, k, 2, more=k < 7)
            copy_out(B - 2, 6, 0)
            copy_out(B - 2, 7, 1)

            def arrived2(job):
                arrived(act, job, JOBS2, full2)

            for h in range(2):
                arrived2(f"oT{h}")
                if h == 0:
                    act.wait_ge(pv_done, UNITS)
                a.activation(o1T[:, h * 512:(h + 1) * 512], bank(f"oT{h}", JOBS2), ACT.Copy).then_inc(o1T_done, 1)
            for h in range(2):
                arrived2(f"nT{h}")
                a.activation(n3T[:, h * 512:(h + 1) * 512], bank(f"nT{h}", JOBS2), ACT.Copy).then_inc(n3T_done, 1)
            act.wait_ge(slot_done, 1)

            def step(s, par, there):
                nxt = par ^ 1
                if there(s + 1):
                    act.wait_ge(gu_ready, s + 2)
                    if s >= 1:
                        act.wait_ge(h_done, s)
                    a.activation(eg[:, nxt, :], ps[:, 2 + 2 * nxt, 0:I], ACT.Tanh, scale=0.5).then_inc(eg_done, 1)
                if there(s + 2):
                    act.wait_ge(gT_ready, s + 3)
                    if s >= 0:
                        act.wait_ge(gu_ready, s + 1)
                    a.activation(ginT[:, par, :], ps[:, 0, 0:P], ACT.Copy).then_inc(gT_copied, 1)
                if there(s):
                    act.wait_ge(hT_ready, s + 1)
                    if s >= 2:
                        act.wait_ge(y_ready, s - 1)
                    for n, (at, rows) in enumerate(ITILES):
                        last = a.activation(hT[0:rows, par, n * P:(n + 1) * P], ps[0:rows, 1, n * P:(n + 1) * P], ACT.Copy,
                                            scale=0.5)
                    last.then_inc(hT_copied, 1)

            pipeline(step)

        @block.vector
        def _(dve):
            v = nc.vector
            steps, norms = [0], [0]

            def chain(ins):
                steps[0] += 1
                ins.then_inc(dve_step, 1)
                dve.wait_ge(dve_step, steps[0])


            def layer_norm(t0, t1, done):
                for t in range(t0, t1):
                    last = v.bn_stats(stats[:, t, :], x[:, t, :])
                chain(last)
                for t in range(t0, t1):
                    last = v.bn_aggr(mv[:, t, :], stats[:, t, :])
                chain(last)
                v.tensor_scalar(veps[:, t0:t1], mv[:, t0:t1, 1], EPS, None, ALU.add).then_inc(var_ready, 1)
                norms[0] += 1
                dve.wait_ge(rstd_ready, norms[0])
                for t in range(t0, t1):
                    last = v.tensor_scalar(ln[:, t, :], x[:, t, :], mv[:, t, 0:1], rstd[:, t:t + 1], ALU.subtract, ALU.mult)
                    if (t - t0) % 4 == 3:
                        last.then_inc(done, 1)

            def split(buf):
                f, p = part32[:, buf, :], parts[:, buf]
                chain(v.tensor_copy(p[:, 0, :], f))
                chain(v.tensor_tensor(f, f, p[:, 0, :], ALU.subtract))
                chain(v.tensor_copy(p[:, 1, :], f))
                return v.tensor_tensor(p[:, 2, :], f, p[:, 1, :], ALU.subtract)

            dve.wait_ge(x_in, 16)
            layer_norm(0, TILES, ln_done)
            dve.wait_ge(w_in, 16)
            v.tensor_scalar(omu[:, :], w[:, WCOL["mu_r"][0]:WCOL["mu_r"][0] + 2], -1.0, 1.0, ALU.mult, ALU.add).then_inc(const_bf, 1)
            for b in range(B):
                arrived(dve, f"k0_{b}")
                emptied(v.tensor_copy(k0T[:, b * SK:(b + 1) * SK], bank(f"k0_{b}")), f"k0_{b}")
            dve.wait_ge(m1_in, 16)
            v.tensor_scalar(m1b, m1i, 0.0, -BIG, ALU.is_equal, ALU.mult).then_inc(m1_conv, 1)
            dve.wait_ge(m1k_in, 16)
            v.tensor_scalar(m1kb, m1ki, 0.0, -BIG, ALU.is_equal, ALU.mult).then_inc(m1k_conv, 1)
            n = B * H0 * QT
            for u in range(n + 2):
                if u < n:
                    b, h, q = u // 4, u // 2 % 2, u % 2
                    arrived(dve, f"S{u}")
                    dve.wait_ge(m0_conv, b + 1)
                    if u >= 4:
                        arrived(dve, f"T{u - 4}")
                    ins = v.tensor_tensor_reduce(out=pr0[:, u % 4, :], in0=bank(f"S{u}"),
                                                 in1=m0b[:, (QT * b + q) * SK:(QT * b + q + 1) * SK], scale=1.0,
                                                 scalar=float("-3e38"), op0=ALU.add, op1=ALU.max, accum_out=mx0[:, u:u + 1])
                    emptied(ins, f"S{u}")
                    copied(dve, f"S{u}")
                    v.tensor_scalar(nm0[:, u:u + 1], mx0[:, u:u + 1], -float(D0) ** -0.5, None, ALU.mult).then_inc(negmax0, 1)
                w1 = u - 1
                if 0 <= w1 < n:
                    dve.wait_ge(exp0, w1 + 1)
                    v.reciprocal(rd0[:, w1:w1 + 1], den0[:, w1:w1 + 1]).then_inc(inv0, 1)
                    if w1 % 2 == 1:
                        b, h, q = w1 // 4, w1 // 2 % 2, w1 % 2
                        arrived(dve, f"T{w1}")
                        if w1 == 1:
                            dve.wait_ge(m1_conv, 1)
                        if b >= 2:
                            arrived(dve, f"PV{b - 2}")
                        emptied(v.tensor_copy(pt0[:, b % 2, h, :, q * P:(q + 1) * P],
                                              bank(f"T{w1}").rearrange("p (t q) -> p t q", t=KT)), f"T{w1}")
                if u % 4 == 1 and u < n:
                    b = u // 4
                    arrived(dve, f"K{b}")
                    if b >= 2:
                        dve.wait_ge(k_wr, 16 * SPLIT * (b - 1))
                    ins = v.tensor_scalar(part32[:, b % 2, :], bank(f"K{b}"), W("bK"), None, ALU.add)
                    emptied(ins, f"K{b}")
                    copied(dve, f"K{b}")
                    split(b % 2).then_inc(k_split, 1)
                    arrived(dve, f"V{b}")
                    emptied(v.tensor_tensor(v1[:, b * KT:(b + 1) * KT, :], bank(f"V{b}").rearrange("p (t c) -> p t c", t=KT),
                                            W("bV").unsqueeze(1).broadcast_to([P, KT, D]), ALU.add), f"V{b}")
                if u % 2 == 0 and u < n:
                    if u == 0:
                        dve.wait_ge(m1_conv, 1)
                    v.reduce_max(anym[:, 0, u // 2:u // 2 + 1], m1b[:, u // 2, :], AX_X).then_inc(diag_done, 1)
            dve.wait_ge(diag_done, TILES)
            chain(v.tensor_scalar(anym[:, 1, :], anym[:, 0, :], 0.0, None, ALU.is_equal))
            dve.wait_ge(const_bf, 4)
            arrived(dve, f"PV{B - 1}")
            for t in range(TILES):
                v.tensor_scalar(diag[:, t, :], identB, anym[:, 1, t:t + 1], None, ALU.mult).then_inc(diag_done, 1)
            dve.wait_ge(m1k_conv, 1)
            v.memset(ln2T[:, :, 0:1], 0.0).then_inc(xr_done, 1)
            for h in range(2):
                arrived(dve, f"wo{h}")
                xs = x[:, 4 * h:4 * h + 4, :]
                emptied(v.tensor_tensor(xs, xs, bank(f"wo{h}").rearrange("p (t c) -> p t c", t=4), ALU.add), f"wo{h}")
                copied(dve, f"wo{h}")
                layer_norm(4 * h, 4 * h + 4, ln_done)
            for h in range(2):
                copied(dve, f"l2T{h}")
                cur, pre = ln2T[:, 2 * h:2 * h + 2, 1:257], ln2T[:, 2 * h:2 * h + 2, 0:256]
                half = slice(h * 512, (h + 1) * 512)
                for dst, m, done in ((xkT, 1, xk_done), (xrT, 0, xr_done)):
                    mu = w[:, WCOL["mu_r"][0] + m:WCOL["mu_r"][0] + m + 1]
                    chain(v.tensor_scalar(prv, pre, omu[:, m:m + 1], None, ALU.mult))
                    v.scalar_tensor_tensor(dst[:, half].rearrange("p (b q) -> p b q", b=2), cur, mu, prv,
                                           ALU.mult, ALU.add).then_inc(done, 1)
                    dve.wait_ge(done, h + 1 + (m == 0))
            for h in range(2):
                copied(dve, f"rr{h}")
                sg, xs = sig[:, 4 * h:4 * h + 4, :], x[:, 4 * h:4 * h + 4, :]
                chain(v.tensor_scalar(sg, sg, 1.0, None, ALU.add))
                chain(v.reciprocal(sg, sg))
                arrived(dve, f"vv{h}")
                ins = v.tensor_tensor(sg, sg, bank(f"vv{h}").rearrange("p (t c) -> p t c", t=4), ALU.mult)
                emptied(ins, f"vv{h}")
                copied(dve, f"vv{h}")
                chain(v.tensor_tensor(xs, xs, sg, ALU.add))
                layer_norm(4 * h, 4 * h + 4, ln_done)
            for h in range(2):
                arrived(dve, f"Q{h}")
                copied(dve, f"F{h}")
                if h == 0:
                    dve.wait_ge(k_wr, 16 * SPLIT * B)
                ins = v.scalar_tensor_tensor(part32[:, h, :], bank(f"Q{h}"), W("bQ"), fq[:, h * 512:(h + 1) * 512], ALU.add, ALU.mult)
                emptied(ins, f"Q{h}")
                copied(dve, f"Q{h}")
                split(h).then_inc(q_split, 1)

            scores_seen = v.alloc_register("scores_seen")

            def maxima(i, k, par):
                u, b, _ = unit(i, k)
                for j in range(GH):
                    for q in range(QT):
                        n = 8 * u + 2 * j + q
                        counted(v, sq_ready, i, n + 1, scores_seen)
                        v.tensor_tensor_reduce(out=junk[:, q, :], in0=ps[:, 4 + q, :], in1=m1s[:, par, q, :],
                                               scale=1.0, scalar=-3e38, op0=ALU.add, op1=ALU.max,
                                               accum_out=mx1[:, par, q, j:j + 1]).then_inc(sq_used, 1)
                dve.wait_ge(sq_used, 8 * u + 8)
                if not (isinstance(i, int) and u < 2):
                    dve.wait_ge(mt_ready, u - 1)
                v.tensor_scalar(nm1[:, par, :, 0, :], mx1[:, par, :, :], -1.0, None, ALU.mult).then_inc(nm_hi, 1)
                dve.wait_ge(nm_hi, u + 1)
                v.scalar_tensor_tensor(nm1[:, par, :, 1, :], mx1[:, par, :, :], -1.0, nm1[:, par, :, 0, :],
                                       ALU.mult, ALU.subtract).then_inc(negmax1, 1)

            def normalise(i, k, par):
                u, b, grp = unit(i, k)
                dve.wait_ge(ot_ready, u + 1)
                src = ps[:, 6 + par, 256:512].rearrange("p (q j c) -> p q j c", q=QT, j=GH)
                v.reciprocal(rden[:, par, :, :], src[:, :, :, D1]).then_inc(rd_done, 1)
                dve.wait_ge(rd_done, u + 1)
                dst = otok[:, bass.ds(QT * b, QT), grp * 32:(grp + 1) * 32].rearrange("p q (j d) -> p q j d", j=GH)
                v.tensor_tensor(dst, src[:, :, :, 0:D1], rden[:, par, :, :].unsqueeze(3).broadcast_to([P, QT, GH, D1]),
                                ALU.mult).then_inc(otok_done, 1)

            maxima(0, 0, 0)
            maxima(0, 1, 1)
            def body(i, k, out=True, more=True):
                if more:
                    maxima(i, k + 2, k % 2)
                if out:
                    normalise(i, k - 2, k % 2)

            body(0, 0, out=False)
            body(0, 1, out=False)
            body(0, 2)
            body(0, 3)
            v.reg_mov(scores_seen, 8 * 6 + 1)
            with v.Fori(0, B - 2) as i:
                for k in range(4, 8):
                    body(i, k)
            for k in range(4, 8):
                body(B - 2, k, more=k < 6)
            normalise(B - 2, 6, 0)
            normalise(B - 2, 7, 1)

            def arrived2(job):
                arrived(dve, job, JOBS2, full2)

            dve.wait_ge(xb_done, 1)
            for h in range(2):
                arrived2(f"wo{h}")
                xs = x[:, 4 * h:4 * h + 4, :]
                chain(v.tensor_tensor(xs, xs, bank(f"wo{h}", JOBS2).rearrange("p (t c) -> p t c", t=4), ALU.add))
                layer_norm(4 * h, 4 * h + 4, lnC_done)
            te = lambda c: rt[:, c:c + 64].rearrange("p (t e) -> p t e", e=E)
            lgv, wv_, hot, t4, t5 = te(0), te(64), te(128), te(192), te(256)
            hotB = rt[:, 320:352].bitcast(BF16)
            c8 = lambda c: rt[:, c:c + 8]
            mxl, mxw, ntile, base, tend, slotf = c8(384), c8(392), c8(400), c8(408), c8(416), c8(424)
            st8 = rt[0:1, 448:448 + SLOT_TILES * E].rearrange("p (s e) -> p s e", e=E)
            ex = rt[0:1, 576:576 + SLOT_TILES]
            bc = lambda ap: ap.unsqueeze(2).broadcast_to([P, TILES, E])
            arrived2("lg")
            chain(v.tensor_copy(lgv, bank("lg", JOBS2)[:, 0:64].rearrange("p (t e) -> p t e", e=E)))
            chain(v.reduce_max(mxl, lgv, AX_X))
            chain(v.tensor_tensor(wv_, lgv, bc(mxl), ALU.is_equal))
            chain(v.tensor_tensor(wv_, wv_, C("rank8").rearrange("p (t e) -> p t e", e=E), ALU.mult))
            chain(v.tensor_tensor(wv_, wv_, C("floor8").rearrange("p (t e) -> p t e", e=E), ALU.max))
            chain(v.reduce_max(mxw, wv_, AX_X))
            chain(v.tensor_tensor(hot, wv_, bc(mxw), ALU.is_equal))
            v.tensor_copy(hotB, rt[:, 128:192]).then_inc(onehot_done, 1)
            arrived2("cnt")
            cnt = rt[:, 432:440]
            chain(v.tensor_copy(cnt, bank("cnt", JOBS2)[:, 0:8]))
            chain(v.tensor_tensor(t4, bc(cnt), C("thresholds").rearrange("p (e j) -> p e j", e=E), ALU.is_gt))
            chain(v.reduce_sum(ntile, t4, AX_X))
            chain(v.tensor_tensor(t4, ntile.unsqueeze(1).broadcast_to([P, E, E]), C("before").rearrange("p (e j) -> p e j", e=E), ALU.mult))
            chain(v.reduce_sum(base, t4, AX_X))
            chain(v.tensor_tensor(tend, base, ntile, ALU.add))
            chain(v.tensor_scalar(base, base, float(P), None, ALU.mult))
            arrived2("pos")
            chain(v.tensor_tensor(t5, bank("pos", JOBS2)[:, 0:64].rearrange("p (t e) -> p t e", e=E),
                                  base.unsqueeze(1).broadcast_to([P, TILES, E]), ALU.add))
            chain(v.tensor_tensor(t5, t5, hot, ALU.mult))
            chain(v.reduce_sum(slotf, t5, AX_X))
            v.tensor_copy(slot_u, slotf).then_inc(slot_done, 1)
            chain(v.tensor_tensor(st8, tend[0:1, :].unsqueeze(1).broadcast_to([1, SLOT_TILES, E]),
                                  C("slot_tile")[0:1, :].rearrange("p (s e) -> p s e", e=E), ALU.is_le))
            chain(v.reduce_sum(ex, st8, AX_X))
            v.tensor_scalar(experts, ex, float(E - 1), None, ALU.min).then_inc(experts_done, 1)

            def step(s, par, there):
                nxt = par ^ 1
                if there(s + 1):
                    dve.wait_ge(eg_done, s + 2)
                    v.scalar_tensor_tensor(eg[:, nxt, :], eg[:, nxt, :], 1.0, ps[:, 2 + 2 * nxt, 0:I], ALU.add, ALU.mult)\
                        .then_inc(silu_done, 1)
                    if s >= 1:
                        dve.wait_ge(hT_ready, s)
                    dve.wait_ge(silu_done, s + 2)
                    v.tensor_tensor(hh[:, nxt, :], ps[:, 3 + 2 * nxt, 0:I], eg[:, nxt, :], ALU.mult).then_inc(h_done, 1)
                if there(s - 1):
                    dve.wait_ge(y_ready, s)
                    if s >= 3:
                        dve.wait_ge(ys_out[nxt], 16 * ((s - 1) // 2))
                    v.tensor_copy(yo[:, nxt, :], ps[:, 6, 0:P]).then_inc(y_copied, 1)

            pipeline(step)
            dve.wait_ge(yg_in, 16 * TILES)
            v.tensor_tensor(x, x, yg, ALU.add).then_inc(fin_done, 1)

        @block.tensor
        def _(pe):
            m = nc.tensor

            def transposes(job, src, n, jobs=JOBS):
                for t in range(n):
                    last = m.transpose(bank(job, jobs)[:, t * P:(t + 1) * P], src(t), ident)
                return last

            pe.wait_ge(c_in, 16)
            for h in range(2):
                pe.wait_ge(ln_done, h + 1)
                filled(transposes(f"lnT{h}", lambda t: ln[:, 4 * h + t, :], 4), f"lnT{h}")
            pe.wait_ge(w_in, 16)
            for h in range(2):
                copied(pe, f"lnT{h}")
                filled(m.matmul(bank(f"q{h}"), W("Wq0"), lnT[:, h * 512:(h + 1) * 512], start=True, stop=True), f"q{h}")

            def ctx(b):
                return c_raw[:, b * SK:(b + 1) * SK]

            for b in range(B):
                pe.wait_ge(ctx_in[b], 16)
                claim(pe, f"k0_{b}")
                filled(m.matmul(bank(f"k0_{b}"), W("Wk0"), ctx(b), start=True, stop=True), f"k0_{b}")

            def values(job, b, weight):
                claim(pe, job)
                for t in range(KT):
                    last = m.matmul(bank(job)[:, t * P:(t + 1) * P], ctx(b)[:, t * P:(t + 1) * P], W(weight), start=True, stop=True)
                filled(last, job)

            for b in range(B):
                values(f"v0_{b}", b, "Wv0")

            n = B * H0 * QT

            def scores0(u):
                b, h, q = u // 4, u // 2 % 2, u % 2
                job = f"S{u}"
                claim(pe, job)
                copied(pe, f"q{b // 2}")
                copied(pe, f"k0_{b}")
                r = slice(D0 * h, D0 * (h + 1))
                at = b * SQ + q * P
                filled(m.matmul(bank(job), q0T[r, at:at + P], k0T[r, b * SK:(b + 1) * SK], start=True, stop=True), job)

            scores0(0)
            scores0(1)
            for u in range(n + 2):
                if u + 2 < n:
                    scores0(u + 2)
                w1 = u - 1
                if 0 <= w1 < n:
                    claim(pe, f"T{w1}")
                    pe.wait_ge(probs0, w1 + 1)
                    filled(transposes(f"T{w1}", lambda t: pr0[:, w1 % 4, t * P:(t + 1) * P], KT), f"T{w1}")
                if u >= 5 and (u - 5) % 4 == 0:
                    b = (u - 5) // 4
                    job = f"PV{b}"
                    claim(pe, job)
                    for t in range(4):
                        copied(pe, f"T{4 * b + t}")
                    copied(pe, f"v0_{b}")
                    for t in range(KT):
                        for h in range(H0):
                            last = m.matmul(bank(job)[D0 * h:D0 * (h + 1), 0:SQ], v0[:, b * KT + t, D0 * h:D0 * (h + 1)],
                                            pt0[:, b % 2, h, t, :], start=t == 0, stop=t == KT - 1)
                    filled(last, job)
                if u % 4 == 1 and u < n:
                    b = u // 4
                    claim(pe, f"K{b}")
                    filled(m.matmul(bank(f"K{b}"), W("wK"), ctx(b), start=True, stop=True), f"K{b}")
                    values(f"V{b}", b, "wV")
            for h in range(2):
                claim(pe, f"F{h}")
                pe.wait_ge(diag_done, TILES + 4 * h + 4)
                pe.wait_ge(const_bf, 4)
                for t in range(4):
                    last = m.matmul(bank(f"F{h}")[:, t * P:(t + 1) * P], onesB, diag[:, 4 * h + t, :], start=True, stop=True)
                filled(last, f"F{h}")

            def by_token(job, src, weight):
                claim(pe, job)
                for t in range(4):
                    last = m.matmul(bank(job)[:, t * P:(t + 1) * P], src(t), W(weight), start=True, stop=True)
                filled(last, job)

            for h in range(2):
                copied(pe, f"PV{2 * h}")
                copied(pe, f"PV{2 * h + 1}")
                by_token(f"wo{h}", lambda t: lnT[:, (4 * h + t) * P:(4 * h + t + 1) * P], "Wo0")
            for h in range(2):
                claim(pe, f"l2T{h}")
                pe.wait_ge(ln_done, 3 + h)
                filled(transposes(f"l2T{h}", lambda t: ln[:, 4 * h + t, :], 4), f"l2T{h}")
            for h in range(2):
                claim(pe, f"kk{h}")
                pe.wait_ge(xk_done, h + 1)
                filled(m.matmul(bank(f"kk{h}"), W("Wk"), xkT[:, h * 512:(h + 1) * 512], start=True, stop=True), f"kk{h}")
            for h in range(2):
                pe.wait_ge(xr_done, h + 2)
                by_token(f"rr{h}", lambda t: xrT[:, (4 * h + t) * P:(4 * h + t + 1) * P], "Wr")
            for h in range(2):
                pe.wait_ge(kact_done, h + 1)
                by_token(f"vv{h}", lambda t: kact[:, (4 * h + t) * P:(4 * h + t + 1) * P], "Wv")
            for h in range(2):
                claim(pe, f"l3T{h}")
                pe.wait_ge(ln_done, 5 + h)
                filled(transposes(f"l3T{h}", lambda t: ln[:, 4 * h + t, :], 4), f"l3T{h}")
            for h in range(2):
                claim(pe, f"Q{h}")
                copied(pe, f"l3T{h}")
                filled(m.matmul(bank(f"Q{h}"), W("wQ"), ln3T[:, h * 512:(h + 1) * 512], start=True, stop=True), f"Q{h}")

            R = MROWS + ROWS

            def scores_q(i, k, j):
                u, b, _ = unit(i, k)
                if j == 0:
                    pe.wait_ge(m1s_done, u + 1)
                for q in range(QT):
                    n = 8 * u + 2 * j + q
                    if not (isinstance(i, int) and n < 2):
                        pe.wait_ge(sq_used, n - 1)
                    m.matmul(ps[:, 4 + q, :], qst[0:R, bass.ds(u * (GH * SQ) + j * SQ + q * P, P)],
                             kst[0:R, bass.ds(u * (GH * SK) + j * SK, SK)], start=True, stop=True).then_inc(sq_ready, 1)

            def scores_k(i, k, j):
                u, b, _ = unit(i, k)
                n = 4 * u + j
                if not (isinstance(i, int) and n < 2):
                    pe.wait_ge(exp1, n - 1)
                for c in range(2):
                    out = ps[:, 2 * (j % 2) + c, :]
                    m.matmul(out, identB, m1kb[:, bass.ds(b * KT + 2 * c, 2), :].rearrange("p t q -> p (t q)"), start=True, stop=False,
                             skip_group_check=True)
                    for t in range(2):
                        last = m.matmul(out[:, t * SQ:(t + 1) * SQ], kst[0:R, bass.ds(u * (GH * SK) + j * SK + (2 * c + t) * P, P)],
                                        qst[0:R, bass.ds(u * (GH * SQ) + j * SQ, SQ)], start=False, stop=True, skip_group_check=True)
                last.then_inc(st_ready, 1)

            def weigh(i, k, par, t):
                u, _, _ = unit(i, k)
                for j in range(GH):
                    last = m.matmul(ps[32 * j:32 * (j + 1), 6 + par, 0:SQ], vst[:, par, t, j, :], pt[:, par, j, t, :],
                                    start=t == 0, stop=t == KT - 1)
                if t == KT - 1:
                    last.then_inc(pv_done, 1)

            def turn_max(i, k, par):
                u, _, _ = unit(i, k)
                pe.wait_ge(negmax1, u + 1)
                out = ps[:, 6 + (par ^ 1), 256:384].bitcast(BF16)
                for q in range(QT):
                    last = m.transpose(out[0:MROWS, q * P:(q + 1) * P], nm1[:, par, q, :, :].rearrange("p a j -> p (a j)"), identB)
                last.then_inc(mt_ready, 1)

            def turn_out(i, k, par):
                u, _, _ = unit(i, k)
                pe.wait_ge(oevac, u + 1)
                for q in range(QT):
                    last = m.transpose(ps[:, 6 + par, 256 + q * P:256 + (q + 1) * P], osb[:, par, q * P:(q + 1) * P], ident)
                last.then_inc(ot_ready, 1)

            def free_everything():
                for k in range(8):
                    used = [n for n in JOBS.values() if n % 8 == k]
                    pe.wait_ge(free[k], len(used))

            free_everything()
            pe.wait_ge(sel_in, 16)
            pe.wait_ge(q_rows0, 1)
            for b in range(B):
                pe.wait_ge(k_in[b], 16)
            pe.wait_ge(q_in[0], 32)
            for j in range(GH):
                scores_q(0, 0, j)
            for j in range(GH):
                scores_q(0, 1, j)
            turn_max(0, 0, 0)
            pe.wait_ge(q_in[1], 32)
            pe.wait_ge(m1k_conv, 1)

            def body(i, k, more=True, prev=True, out=True):
                par = k % 2
                u, _, _ = unit(i, k)
                for j in range(GH):
                    if more:
                        scores_q(i, k + 2, j)
                    if j == 0:
                        if out:
                            pe.wait_ge(oevac, u - 1)
                        if more or k % 4 == 2:
                            turn_max(i, k + 1, par ^ 1)
                        pe.wait_ge(mrows, u + 1)
                    scores_k(i, k, j)
                    if prev:
                        if j == 0:
                            pe.wait_ge(exp1, 4 * u)
                            pe.wait_ge(vst_done, u)
                            if out == "late":
                                pe.wait_ge(otok_done, u - 2)
                        weigh(i, k - 1, par ^ 1, j)
                    if j == 2 and out:
                        if more or k % 4 == 2:
                            pe.wait_ge(mrows, u + 2)
                        turn_out(i, k - 2, par)

            body(0, 0, prev=False, out=False)
            body(0, 1, out=False)
            body(0, 2)
            body(0, 3, out="late")
            with m.Fori(0, B - 2) as i:
                for k in range(4, 8):
                    body(i, k, out="late")
            for k in range(4, 8):
                body(B - 2, k, more=k < 6, out="late")
            pe.wait_ge(exp1, 4 * UNITS)
            pe.wait_ge(vst_done, UNITS)
            pe.wait_ge(otok_done, UNITS - 2)
            for t in range(KT):
                weigh(B - 2, 7, 1, t)
            turn_out(B - 2, 6, 0)
            turn_out(B - 2, 7, 1)

            def ready2(ins, job):
                ins.then_inc(full2[JOBS2[job] % 8], 1)

            pe.wait_ge(otok_done, UNITS)
            for h in range(2):
                ready2(transposes(f"oT{h}", lambda t: otok[:, 4 * h + t, :], 4, JOBS2), f"oT{h}")
            for h in range(2):
                pe.wait_ge(o1T_done, h + 1)
                job = f"wo{h}"
                for t in range(4):
                    c = (4 * h + t) * P
                    last = m.matmul(bank(job, JOBS2)[:, t * P:(t + 1) * P], o1T[:, c:c + P], W("wO"), start=True, stop=True)
                ready2(last, job)
            for h in range(2):
                pe.wait_ge(lnC_done, h + 1)
                ready2(transposes(f"nT{h}", lambda t: ln[:, 4 * h + t, :], 4, JOBS2), f"nT{h}")
            for t in range(TILES):
                pe.wait_ge(n3T_done, t // 4 + 1)
                last = m.matmul(bank("lg", JOBS2)[:, t * E:(t + 1) * E], n3T[:, t * P:(t + 1) * P], W("router"), start=True, stop=True)
            ready2(last, "lg")
            hotB = rt[:, 320:352].bitcast(BF16)
            pe.wait_ge(onehot_done, 1)
            for t in range(TILES):
                last = m.matmul(ps[:, JOBS2["cnt"] % 8, 0:E], onesB, hotB[:, t * E:(t + 1) * E], start=t == 0, stop=t == TILES - 1)
            ready2(last, "cnt")
            pos = bank("pos", JOBS2)[:, 0:TILES * E]
            m.matmul(pos, triB, hotB, start=True, stop=False, skip_group_check=True)
            for t in range(TILES - 1):
                k = TILES - 1 - t
                last = m.matmul(pos[:, (t + 1) * E:].rearrange("p (t e) -> p t e", e=E), onesB,
                                hotB[:, t * E:(t + 1) * E].unsqueeze(1).broadcast_to([P, k, E]), start=False, stop=t == TILES - 2,
                                skip_group_check=True)
            ready2(last, "pos")

            pe.wait_ge(experts_done, 1)
            pe.wait_ge(moe_w_in, 64)
            pe.wait_ge(gin_in, 16)
            pe.wait_ge(slot_done, 1)

            def expert(s):
                return m.value_load(experts[0:1, s:s + 1], min_val=0, max_val=E - 1)

            def step(s, par, there):
                nxt = par ^ 1
                if there(s + 1):
                    e = expert(s + 1)
                    pe.wait_ge(gT_copied, s + 2)
                    if s >= 1:
                        pe.wait_ge(h_done, s)
                    m.matmul(ps[:, 2 + 2 * nxt, 0:I], ginT[:, nxt, :], gu[:, bass.ds(e * (2 * I), I)], start=True, stop=True)
                    m.matmul(ps[:, 3 + 2 * nxt, 0:I], ginT[:, nxt, :], gu[:, bass.ds(e * (2 * I) + I, I)], start=True, stop=True)\
                        .then_inc(gu_ready, 1)
                if there(s + 2):
                    if s >= -1:
                        pe.wait_ge(gT_copied, s + 2)
                    m.transpose(ps[:, 0, 0:P], gin[:, s + 2, :], ident)\
                        .then_inc(gT_ready, 1)
                if there(s):
                    pe.wait_ge(h_done, s + 1)
                    if s >= 1:
                        pe.wait_ge(hT_copied, s)
                    for n, (at, rows) in enumerate(ITILES):
                        last = m.transpose(ps[0:rows, 1, n * P:(n + 1) * P], hh[:, par, at:at + rows], ident)
                    last.then_inc(hT_ready, 1)
                if there(s - 1):
                    e = expert(s - 1)
                    pe.wait_ge(hT_copied, s)
                    if s >= 2:
                        pe.wait_ge(y_copied, s - 1)
                    for n, (at, rows) in enumerate(ITILES):
                        last = m.matmul(ps[:, 6, 0:P], hT[0:rows, nxt, n * P:(n + 1) * P], dn[0:rows, n, bass.ds(e * D, D)],
                                        start=n == 0, stop=n == 2)
                    last.then_inc(y_ready, 1)

            pipeline(step)


def kernel(**inputs):
    import numpy as np
    import concourse.bacc as bacc
    from concourse.bass_utils import run_bass_kernel_spmd

    a = {k: np.asarray(v) for k, v in inputs.items()}

    def by_dim(t):
        return t.reshape(t.shape[0], H1, D1).transpose(0, 2, 1).reshape(t.shape[0], D)

    def col(t):
        return t.reshape(D, 1)

    kv = a["L0_xattn_Wkv"]
    packed = {
        "Wq0": a["L0_xattn_Wq"], "Wk0": kv[:, :D], "Wv0": kv[:, D:], "Wo0": a["L0_xattn_Wo"],
        "Wr": a["L0_ffn_W_r"].T, "Wk": a["L0_ffn_W_k"].T, "Wv": a["L0_ffn_W_v"].T,
        "wQ": by_dim(a["L1_xattn_wQ_w"].T), "wK": by_dim(a["L1_xattn_wK_w"].T), "wV": a["L1_xattn_wV_w"].T,
        "wO": a["L1_xattn_wO_w"].T, "router": a["L1_ffn_router_w"].T,
        "mu_r": col(a["L0_ffn_mu_r"]), "mu_k": col(a["L0_ffn_mu_k"]),
        "bQ": by_dim(a["L1_xattn_wQ_b"].reshape(1, D)).T, "bK": by_dim(a["L1_xattn_wK_b"].reshape(1, D)).T,
        "bV": np.broadcast_to(a["L1_xattn_wV_b"], (P, D)), "bO": np.broadcast_to(a["L1_xattn_wO_b"], (P, D)),
    }
    weights = np.concatenate([packed[n] for n, _ in W_SIZES], axis=1)
    q = np.arange(P)
    const = np.zeros((P, CTOT), np.float32)

    def put(name, value):
        const[:, CCOL[name][0]:CCOL[name][1]] = np.asarray(value, np.float32).reshape(-1, CCOL[name][1] - CCOL[name][0])

    e = np.arange(E)
    put("ident", np.eye(P))
    put("tri", q[:, None] < q[None, :])
    put("rank8", np.tile(E - e, TILES))
    put("floor8", np.tile(e == E - 1, TILES))
    put("thresholds", np.tile(P * e, E))
    put("before", e[None, :] < e[:, None])
    put("slot_tile", np.repeat(np.arange(SLOT_TILES), E))
    select = np.zeros((MROWS, GH, SK // 2), np.uint32)
    for r in range(MROWS):
        select[r, r % GH] = 0x3F803F80

    def rows(t):
        return np.ascontiguousarray(t.reshape(TILES, P, SK).transpose(1, 0, 2)).reshape(P, TILES * SK)

    m1 = a["mask_Bx1xSxS2_ik1"].reshape(B, SQ, SK)
    arrays = {
        "x_dram": a["x"].reshape(TOK, D),
        "ctxT_dram": a["ctx_1024"].reshape(B * SK, D).T,
        "mask0_dram": rows(a["mask_BxSxS2_bf1"].view(np.uint8)),
        "mask1_dram": rows(m1).reshape(P, TILES, SK),
        "mask1k_dram": m1.transpose(0, 2, 1).reshape(B * KT, P, SQ).transpose(1, 0, 2),
        "weights_dram": weights,
        "gate_up_dram": np.concatenate([a["L1_ffn_gate_w"], a["L1_ffn_up_w"]], axis=1).transpose(2, 0, 1).reshape(D, E * 2 * I),
        "down_dram": a["L1_ffn_down_w"].transpose(2, 0, 1).reshape(I, E * D),
        "const_dram": const,
        "select_dram": select.reshape(MROWS, GH * SK // 2).view(np.float32),
    }
    arrays = {k: np.ascontiguousarray(t) for k, t in arrays.items()}
    nc = bacc.Bacc("TRN2", target_bir_lowering=False, num_devices=1)
    args = [nc.dram_tensor(k, t.shape, mybir.dt.from_np(t.dtype), kind="ExternalInput").ap() for k, t in arrays.items()]
    out = nc.dram_tensor("out_dram", (TOK, D), F32, kind="ExternalOutput").ap()
    build(nc, *args, out)
    r = run_bass_kernel_spmd(nc, [arrays], core_ids=[0])
    return r.results[0]["out_dram"].reshape(B, SQ, D)
```
